# Optimizing a Trainium2 kernel written in Bass

```python
import numpy as np
import jax
import jax.numpy as jnp

def _softmax(x, axis=-1):
    return jax.nn.softmax(x, axis=axis)

def _gelu(x):
    return jax.nn.gelu(x, approximate=True)

def _silu(x):
    return jax.nn.silu(x)

def _sigmoid(x):
    return jax.nn.sigmoid(x)

def _layernorm(x, axis=-1, eps=1e-05):
    m = jnp.mean(x, axis=axis, keepdims=True)
    v = jnp.var(x, axis=axis, keepdims=True)
    return (x - m) / jnp.sqrt(v + eps)

def _scatter_add(tgt, idx, src, axis=0):
    return tgt.at[idx].add(src)

def _segment_sum(src, seg, n):
    return jax.ops.segment_sum(src, seg, n)
kernel_name = 'mk_rec_standalone_d1_rec_r8_9dac78'

def setup_inputs(seed: int=0):
    np.random.seed(seed)
    _w = jnp.asarray

    def _rec_inputs():
        import jax
        import jax.numpy as jnp
        _rk = jax.random.key(seed)
        r_cont_feats = -0.000692196 + 0.998807 * jax.random.normal(jax.random.fold_in(_rk, 1), (2048, 13), jnp.float32)
        r_cat_feats = jnp.stack([jax.random.randint(jax.random.fold_in(jax.random.fold_in(_rk, 2), 0), (2048,), 0, 99999, jnp.int32), jax.random.randint(jax.random.fold_in(jax.random.fold_in(_rk, 2), 1), (2048,), 0, 12499, jnp.int32), jax.random.randint(jax.random.fold_in(jax.random.fold_in(_rk, 2), 2), (2048,), 4, 99997, jnp.int32), jax.random.randint(jax.random.fold_in(jax.random.fold_in(_rk, 2), 3), (2048,), 2, 99997, jnp.int32), jax.random.randint(jax.random.fold_in(jax.random.fold_in(_rk, 2), 4), (2048,), 1, 99988, jnp.int32), jax.random.randint(jax.random.fold_in(jax.random.fold_in(_rk, 2), 5), (2048,), 1, 99996, jnp.int32), jax.random.randint(jax.random.fold_in(jax.random.fold_in(_rk, 2), 6), (2048,), 12, 99997, jnp.int32), jax.random.randint(jax.random.fold_in(jax.random.fold_in(_rk, 2), 7), (2048,), 17, 99995, jnp.int32), jax.random.randint(jax.random.fold_in(jax.random.fold_in(_rk, 2), 8), (2048,), 0, 99998, jnp.int32), jax.random.randint(jax.random.fold_in(jax.random.fold_in(_rk, 2), 9), (2048,), 0, 99998, jnp.int32), jax.random.randint(jax.random.fold_in(jax.random.fold_in(_rk, 2), 10), (2048,), 3, 99993, jnp.int32), jax.random.randint(jax.random.fold_in(jax.random.fold_in(_rk, 2), 11), (2048,), 0, 99993, jnp.int32), jax.random.randint(jax.random.fold_in(jax.random.fold_in(_rk, 2), 12), (2048,), 1, 99988, jnp.int32), jax.random.randint(jax.random.fold_in(jax.random.fold_in(_rk, 2), 13), (2048,), 0, 99997, jnp.int32), jax.random.randint(jax.random.fold_in(jax.random.fold_in(_rk, 2), 14), (2048,), 3, 99993, jnp.int32), jax.random.randint(jax.random.fold_in(jax.random.fold_in(_rk, 2), 15), (2048,), 10, 99994, jnp.int32), jax.random.randint(jax.random.fold_in(jax.random.fold_in(_rk, 2), 16), (2048,), 10, 99998, jnp.int32), jax.random.randint(jax.random.fold_in(jax.random.fold_in(_rk, 2), 17), (2048,), 18, 99979, jnp.int32), jax.random.randint(jax.random.fold_in(jax.random.fold_in(_rk, 2), 18), (2048,), 1, 99996, jnp.int32), jax.random.randint(jax.random.fold_in(jax.random.fold_in(_rk, 2), 19), (2048,), 6, 99987, jnp.int32), jax.random.randint(jax.random.fold_in(jax.random.fold_in(_rk, 2), 20), (2048,), 6, 12500, jnp.int32), jax.random.randint(jax.random.fold_in(jax.random.fold_in(_rk, 2), 21), (2048,), 2, 12500, jnp.int32), jax.random.randint(jax.random.fold_in(jax.random.fold_in(_rk, 2), 22), (2048,), 7, 12498, jnp.int32), jax.random.randint(jax.random.fold_in(jax.random.fold_in(_rk, 2), 23), (2048,), 2, 99999, jnp.int32), jax.random.randint(jax.random.fold_in(jax.random.fold_in(_rk, 2), 24), (2048,), 29, 99990, jnp.int32), jax.random.randint(jax.random.fold_in(jax.random.fold_in(_rk, 2), 25), (2048,), 10, 99986, jnp.int32)], axis=1)
        return (r_cont_feats, r_cat_feats)
    r_cont_feats, r_cat_feats = _rec_inputs()

    def _L0_rec_setup():
        import jax, jax.numpy as jnp
        import numpy as np
        B, F_CAT, F_CONT, V, D = (2048, 26, 13, 12500, 64)
        H1, H2 = (1024, 512)
        IN_DIM = (F_CAT + F_CONT) * D
        BN_EPS = 1e-05

        def _batchnorm(x, g, b):
            mu = jnp.mean(x, axis=0)
            var = jnp.mean((x - mu) ** 2, axis=0)
            return g * (x - mu) * jax.lax.rsqrt(var + BN_EPS) + b
        key = jax.random.key(seed)
        ks = jax.random.split(key, 20)
        s = 0.05
        return {'cat_feats': jax.random.randint(ks[0], (B, F_CAT), 0, V), 'cont_feats': jax.random.normal(ks[1], (B, F_CONT), jnp.float32), 'bias': jax.random.normal(ks[2], (1,), jnp.float32), 'cat_t1': jax.random.normal(ks[3], (F_CAT, V), jnp.float32) * s, 'cat_t2': jax.random.normal(ks[4], (F_CAT, V, D), jnp.float32) * s, 'cont_t1': jax.random.normal(ks[5], (F_CONT,), jnp.float32) * s, 'cont_t2': jax.random.normal(ks[6], (F_CONT, D), jnp.float32) * s, 'W1': jax.random.normal(ks[7], (IN_DIM, H1), jnp.float32) * (1.0 / np.sqrt(IN_DIM)), 'b1': jnp.zeros((H1,), jnp.float32), 'g1': jnp.ones((H1,), jnp.float32), 'be1': jnp.zeros((H1,), jnp.float32), 'W2': jax.random.normal(ks[8], (H1, H2), jnp.float32) * (1.0 / np.sqrt(H1)), 'b2': jnp.zeros((H2,), jnp.float32), 'g2': jnp.ones((H2,), jnp.float32), 'be2': jnp.zeros((H2,), jnp.float32), 'W3': jax.random.normal(ks[9], (H2, 1), jnp.float32) * (1.0 / np.sqrt(H2)), 'b3': jnp.zeros((1,), jnp.float32)}
    _L0_rec_all = _L0_rec_setup()
    _L0_rec_in = {k: v for k, v in _L0_rec_all.items() if k in ('bias', 'cat_t1', 'cat_t2', 'cont_t1', 'cont_t2', 'W1', 'b1', 'g1', 'be1', 'W2', 'b2', 'g2', 'be2', 'W3', 'b3')}
    del _L0_rec_all
    return {'r_cont_feats': r_cont_feats, 'r_cat_feats': r_cat_feats, 'L0_rec_bias': _L0_rec_in['bias'], 'L0_rec_cat_t1': _L0_rec_in['cat_t1'], 'L0_rec_cat_t2': _L0_rec_in['cat_t2'], 'L0_rec_cont_t1': _L0_rec_in['cont_t1'], 'L0_rec_cont_t2': _L0_rec_in['cont_t2'], 'L0_rec_W1': _L0_rec_in['W1'], 'L0_rec_b1': _L0_rec_in['b1'], 'L0_rec_g1': _L0_rec_in['g1'], 'L0_rec_be1': _L0_rec_in['be1'], 'L0_rec_W2': _L0_rec_in['W2'], 'L0_rec_b2': _L0_rec_in['b2'], 'L0_rec_g2': _L0_rec_in['g2'], 'L0_rec_be2': _L0_rec_in['be2'], 'L0_rec_W3': _L0_rec_in['W3'], 'L0_rec_b3': _L0_rec_in['b3']}

def reference(r_cont_feats, r_cat_feats, L0_rec_bias, L0_rec_cat_t1, L0_rec_cat_t2, L0_rec_cont_t1, L0_rec_cont_t2, L0_rec_W1, L0_rec_b1, L0_rec_g1, L0_rec_be1, L0_rec_W2, L0_rec_b2, L0_rec_g2, L0_rec_be2, L0_rec_W3, L0_rec_b3):
    import jax
    import jax.numpy as jnp

    def _L0_rec_ref(cat_feats, cont_feats, bias, cat_t1, cat_t2, cont_t1, cont_t2, W1, b1, g1, be1, W2, b2, g2, be2, W3, b3):
        import jax, jax.numpy as jnp
        import numpy as np
        B, F_CAT, F_CONT, V, D = (2048, 26, 13, 12500, 64)
        H1, H2 = (1024, 512)
        IN_DIM = (F_CAT + F_CONT) * D
        BN_EPS = 1e-05

        def _batchnorm(x, g, b):
            mu = jnp.mean(x, axis=0)
            var = jnp.mean((x - mu) ** 2, axis=0)
            return g * (x - mu) * jax.lax.rsqrt(var + BN_EPS) + b
        fidx = jnp.arange(F_CAT)[None, :]
        first_cat = cat_t1[fidx, cat_feats]
        first_cont = cont_t1[None, :] * cont_feats
        fm_first = jnp.sum(first_cat, axis=1) + jnp.sum(first_cont, axis=1)
        emb_cat = cat_t2[fidx, cat_feats]
        emb_cont = cont_t2[None, :, :] * cont_feats[:, :, None]
        E = jnp.concatenate([emb_cat, emb_cont], axis=1)
        s = jnp.sum(E, axis=1)
        fm_second = 0.5 * jnp.sum(s * s - jnp.sum(E * E, axis=1), axis=1)
        deep = E.reshape(E.shape[0], -1)
        h = jax.nn.relu(_batchnorm(deep @ W1 + b1, g1, be1))
        h = jax.nn.relu(_batchnorm(h @ W2 + b2, g2, be2))
        deep_out = (h @ W3 + b3)[:, 0]
        out_pos = jax.nn.sigmoid(bias + fm_first + fm_second + deep_out)[:, None]
        return jnp.concatenate([1.0 - out_pos, out_pos], axis=1)
    y = _L0_rec_ref(r_cat_feats, r_cont_feats, L0_rec_bias, L0_rec_cat_t1, L0_rec_cat_t2, L0_rec_cont_t1, L0_rec_cont_t2, L0_rec_W1, L0_rec_b1, L0_rec_g1, L0_rec_be1, L0_rec_W2, L0_rec_b2, L0_rec_g2, L0_rec_be2, L0_rec_W3, L0_rec_b3)
    return y

_drawn_inputs = setup_inputs


def setup_inputs(seed=0):
    import zlib

    import numpy as np

    out = dict(_drawn_inputs(seed))
    spreads = {'L0_rec_b1': (0.0, 0.8),
     'L0_rec_g1': (1.0, 0.558),
     'L0_rec_be1': (0.0, 0.729),
     'L0_rec_b2': (0.0, 0.8),
     'L0_rec_g2': (1.0, 0.6),
     'L0_rec_be2': (0.0, 0.8)}
    factors = {}
    for name, (base, spread) in spreads.items():
        noise = np.random.default_rng([zlib.crc32(name.encode()), seed]).standard_normal(out[name].shape)
        drawn = base * np.exp(spread * noise) if base else spread * noise
        out[name] = jnp.asarray(drawn.astype(out[name].dtype))
    for name, factor in factors.items():
        out[name] = (out[name] * factor).astype(out[name].dtype)
    return out
```

```python
from contextlib import ExitStack

import concourse.bass as bass
from concourse import mybir

BATCH, CAT, CONT, VOCAB, DIM = 2048, 26, 13, 12500, 64
H1, H2 = 1024, 512
P = 128
EPS = 1e-5

TILES = BATCH // P
BT = 2
BLOCKS = TILES // BT
BC = BT * P
KT = CAT // 2
ROW = DIM + 1
PAIR = 2 * ROW
GROUPS = [(0, 4), (4, 8), (8, KT)]
C1 = H1 // P
C2 = H2 // P
ACC_BANKS = C1 * BC // 512
XT = 4
TP = 3
CONT_KT = -(-CONT // 2)
NB2 = 512
N2 = BATCH // NB2

EMPTY = 1
FM_STEPS = 8
PAR = 3 * C1 + 4 * C2 + 2


def build(nc, table, cat, cont_t, cont_tab, cont_diag, w1, w2, params, out):
    f32, f32r = mybir.dt.float32, mybir.dt.float32r
    i32, bf16 = mybir.dt.int32, mybir.dt.bfloat16
    ACT, ALU, AX = mybir.ActivationFunctionType, mybir.AluOpType, mybir.AxisListType
    ds = bass.ds

    base = -(-nc.sbuf_base // 32) * 32
    cursor = [base]

    def place(name, shape, dtype, size=4):
        n = size
        for d in shape[1:]:
            n *= d
        t = nc.alloc_sbuf_tensor_at(name, shape, dtype, offset=cursor[0])
        cursor[0] += -(-n // 32) * 32
        assert cursor[0] <= nc.sbuf_usable_end, (name, cursor[0])
        return t

    w1hi_at = cursor[0]
    w1hi = place("w1hi", [P, KT, H1], f32r)
    w1lo_at = cursor[0]
    w1lo = place("w1lo", [P, KT, H1], f32r)
    h1 = place("h1", [P, C1, BATCH], f32)
    emb = place("emb", [P, BT, KT * PAIR], f32)
    xhi = place("xhi", [P, XT, BC], f32r)
    xlo = place("xlo", [P, XT, BC], f32r)
    m_sb = place("m_sb", [CONT, H1], f32)
    cont_sb = place("cont_sb", [CONT, BC], f32)
    cont_sq = place("cont_sq", [CONT, BC], f32)
    ctab = place("ctab", [CONT, ROW], f32)
    ctab_sq = place("ctab_sq", [CONT, DIM], f32)
    cnorm = place("cnorm", [CONT, 1], f32)
    diag = place("diag", [P, CONT_KT * CONT], f32)
    idx_all = place("idx_all", [P, (TILES + BT) * CAT], i32)
    idx_off = place("idx_off", [P, CAT], i32)
    idx_now = place("idx_now", [P, BT, CAT], i32)
    ident = place("ident", [P, P], f32)
    par = place("par", [P, PAR], f32)
    part = place("part", [P, len(GROUPS), BT * PAIR], f32)
    junk = place("junk", [P, (KT - 8) * P], bf16, 2)
    tot = place("tot", [P, BT, PAIR], f32)
    ssum = place("ssum", [P, BT, DIM], f32)
    ssum_sq = place("ssum_sq", [P, BT, DIM], f32)
    lin0 = place("lin0", [P, BT], f32)
    lin1 = place("lin1", [P, BT], f32)
    lin = place("lin", [P, TILES], f32)
    ssq = place("ssq", [P, TILES], f32)
    esq = place("esq", [P, TILES, len(GROUPS)], f32)
    eps = place("eps", [P, 1], f32)
    warm = place("warm", [P, 1], f32)
    stats1 = place("stats1", [P, C1, BLOCKS, 6], f32)
    mv1 = place("mv1", [P, C1, 2], f32)
    bn1 = place("bn1", [P, 5, C1], f32)

    kt_bytes = H1 * 4
    w2raw = nc.alloc_sbuf_tensor_at("w2raw", [P, C1, H2], f32, offset=w1hi_at)
    w2hi = nc.alloc_sbuf_tensor_at("w2hi", [P, C1, H2], f32r, offset=w1lo_at)
    w2lo = nc.alloc_sbuf_tensor_at("w2lo", [P, C1, H2], f32r, offset=w1lo_at + 4 * kt_bytes)
    hhi = nc.alloc_sbuf_tensor_at("hhi", [P, C1, NB2], f32r, offset=w1hi_at + 4 * kt_bytes)
    hlo = nc.alloc_sbuf_tensor_at("hlo", [P, C1, NB2], f32r, offset=w1lo_at + 8 * kt_bytes)
    hfull = nc.alloc_sbuf_tensor_at("hfull", [P, 2, NB2], f32, offset=w1hi_at + 8 * kt_bytes)
    cursor[0] = w1hi_at + 9 * kt_bytes
    esq_sum = place("esq_sum", [P, TILES], f32)
    fm_a = place("fm_a", [P, TILES], f32)
    fm_b = place("fm_b", [P, TILES], f32)
    fm = place("fm", [P, TILES], f32)
    stats2 = place("stats2", [P, C2, N2, 6], f32)
    mv2 = place("mv2", [P, C2, 2], f32)
    bn2 = place("bn2", [P, 5, C2], f32)
    zsum = place("zsum", [P, TILES], f32)
    prob = place("prob", [P, TILES, 2], f32)
    W2RAW_KT, W2LO_KT = 3, 7

    raw = h1[:, :, :].rearrange("p c (s n) -> p (c s) n", n=H1)
    RAW_SLOTS = C1 * BATCH // H1

    def raw_slot(k):
        return CONT_KT + k if k < RAW_SLOTS - CONT_KT else k - (RAW_SLOTS - CONT_KT)

    b1, g1, be1 = (par[:, i * C1:(i + 1) * C1] for i in range(3))
    b2, g2, be2, w3 = (par[:, 3 * C1 + i * C2:3 * C1 + (i + 1) * C2] for i in range(4))
    bias_col, b3_col = par[:, PAR - 2:PAR - 1], par[:, PAR - 1:PAR]

    with ExitStack() as ctx:
        bank = [ctx.enter_context(nc.psum_tensor(f"bank{i}", [P, 512], f32)) for i in range(8)]
        acc = [bank[c * BC // 512][:, c * BC % 512:c * BC % 512 + BC] for c in range(C1)]
        tp = [bank[ACC_BANKS + i][:, 0:BC] for i in range(TP)]
        misc = bank[7][:, 0:BT * 128].rearrange("p (j c) -> p j c", j=BT)

        def sem(name):
            return ctx.enter_context(nc.semaphore(name))

        idx_in, par_in, diag_in, ctab_in = sem("idx_in"), sem("par_in"), sem("diag_in"), sem("ctab_in")
        wc_in = sem("wc_in")
        raw_in = [sem(f"raw_in{k}") for k in range(KT)]
        cont_in = sem("cont_in")
        off_made, ident_zero, ident_made = sem("off_made"), sem("ident_zero"), sem("ident_made")
        idx_step = sem("idx_step")
        idx_ready = [sem(f"idx_ready{g}") for g in range(len(GROUPS))]
        gathered = [sem(f"gathered{k}") for k in range(KT)]
        group_open = sem("group_open")
        m_done, m_ready = sem("m_done"), sem("m_ready")
        cnorm_ready, cont_sq_ready, cont_used = sem("cnorm_ready"), sem("cont_sq_ready"), sem("cont_used")
        w1hi_ready, w1_ready = sem("w1hi_ready"), sem("w1_ready")
        transposed, xhi_ready = sem("transposed"), sem("xhi_ready")
        split_done = [sem(f"split_done{s}") for s in range(TP)]
        x_used = [sem(f"x_used{s}") for s in range(XT)]
        acc_full = sem("acc_full")
        acc_free = [sem(f"acc_free{m}") for m in range(ACC_BANKS)]
        squared = [sem(f"squared{g}") for g in range(len(GROUPS))]
        summed = [sem(f"summed{g}") for g in range(len(GROUPS))]
        misc_full = sem("misc_full")
        fm_step = sem("fm_step")
        stats1_done = sem("stats1_done")
        bn1_step, std1_ready = sem("bn1_step"), sem("std1_ready")
        eps_ready = sem("eps_ready")
        w2_in, w2hi_ready, w2_ready = sem("w2_in"), sem("w2hi_ready"), sem("w2_ready")
        h_ready, h_split = sem("h_ready"), sem("h_split")
        h_used = [sem(f"h_used{k}") for k in range(C1 - 1)]
        acc2_full, acc2_free = sem("acc2_full"), sem("acc2_free")
        bn2_step, std2_ready = sem("bn2_step"), sem("std2_ready")
        fin_step = sem("fin_step")
        out_act, out_dve = sem("out_act"), sem("out_dve")
        logit_ready, z_ready, prob_ready, neg_ready = (
            sem("logit_ready"), sem("z_ready"), sem("prob_ready"), sem("neg_ready"))
        out_done = sem("out_done")

        TP_USES = [len(range(s, KT, TP)) for s in range(TP)]
        X_USES = [len(range(s, KT - 1, XT)) for s in range(XT)]

        block = ctx.enter_context(nc.Block())

        @block.sync
        def _(sp):
            sp.dma_start(idx_all[:, 0:TILES * CAT], cat).then_inc(idx_in, 16)
            rows = w1[CAT * DIM:, :]
            whole = (CONT_KT - 1) * P
            sp.dma_start(raw[:, 0:CONT_KT - 1, :],
                         rows[0:whole, :].rearrange("(j p) n -> p j n", p=P)).then_inc(wc_in, 16)
            sp.dma_start(raw[0:DIM, CONT_KT - 1, :], rows[whole:whole + DIM, :]).then_inc(wc_in, 16)
            for k in range(KT):
                if k == RAW_SLOTS - CONT_KT:
                    sp.wait_ge(m_done, 1)
                sp.dma_start(raw[:, raw_slot(k), :], w1[k * P:(k + 1) * P, :]).then_inc(raw_in[k], 16)
            with sp.Fori(0, BLOCKS) as b:
                sp.wait_ge(cont_used, b + EMPTY)
                sp.dma_start(cont_sb[:, :], cont_t[:, ds(b * BC, BC)]).then_inc(cont_in, 16)
            s = W2RAW_KT % XT
            sp.wait_ge(x_used[s], X_USES[s] * (BLOCKS - 1) + W2RAW_KT // XT + 1 + EMPTY)
            for k in range(C1):
                sp.dma_start(w2raw[:, k, :], w2[k * P:(k + 1) * P, :]).then_inc(w2_in, 16)
            sp.wait_ge(neg_ready, 1)
            sp.wait_ge(prob_ready, 1)
            sp.dma_start(out, prob[:, :, :].rearrange("p t c -> p (t c)")).then_inc(out_done, 16)
            sp.wait_ge(out_done, 16)

        @block.gpsimd
        def _(pool):
            nc.gpsimd.iota(idx_off[:, :], pattern=[[VOCAB, CAT]], base=0,
                           channel_multiplier=0).then_inc(off_made, 1)
            nc.gpsimd.memset(ident[:, :], 1.0).then_inc(ident_zero, 1)
            pool.wait_ge(ident_zero, 1)
            nc.gpsimd.affine_select(out=ident[:, :], in_=ident[:, :], compare_op=ALU.is_equal, fill=0.0,
                                    base=0, pattern=[[-1, P]], channel_multiplier=1).then_inc(ident_made, 1)
            with pool.Fori(0, BLOCKS) as b:
                for g, (k0, k1) in enumerate(GROUPS):
                    pool.wait_ge(idx_ready[g], b + 1)
                    pool.wait_ge(summed[g], b + EMPTY)
                    pool.wait_ge(squared[g], BT * b + EMPTY)
                    pool.sem_inc(group_open, 1)
                    for k in range(k0, k1):
                        for j in range(BT):
                            for half in range(2):
                                at = k * PAIR + half * ROW
                                f = 2 * k + half
                                nc.gpsimd.indirect_dma_start(
                                    out=emb[:, j, at:at + ROW], out_offset=None, in_=table,
                                    in_offset=bass.IndirectOffsetOnAxis(ap=idx_now[:, j, f:f + 1], axis=0),
                                ).then_inc(gathered[k], 16)
            for k in range(C1):
                if k == 0:
                    pool.wait_ge(w2_in, 16 * C1)
                nc.gpsimd.tensor_copy(w2hi[:, k, :], w2raw[:, k, :]).then_inc(w2hi_ready, 1)
                if k == 0:
                    s = W2LO_KT % XT
                    pool.wait_ge(x_used[s], X_USES[s] * (BLOCKS - 1) + W2LO_KT // XT + 1 + EMPTY)
                pool.wait_ge(w2hi_ready, k + 1)
                nc.gpsimd.tensor_tensor(w2lo[:, k, :], w2raw[:, k, :], w2hi[:, k, :].bitcast(f32),
                                        ALU.subtract).then_inc(w2_ready, 1)

        @block.scalar
        def _(act):
            for free in (*squared, *acc_free):
                act.sem_inc(free, EMPTY)
            act.dma_start(diag[:, :], cont_diag).then_inc(diag_in, 16)
            act.dma_start(ctab[:, :], cont_tab).then_inc(ctab_in, 16)
            act.dma_start(par[:, :], params).then_inc(par_in, 16)
            act.wait_ge(ctab_in, 16)
            nc.scalar.activation(ctab_sq[:, :], ctab[:, 0:DIM], ACT.Square,
                                 accum_out=cnorm[:, :]).then_inc(cnorm_ready, 1)
            for k in range(KT):
                act.wait_ge(raw_in[k], 16)
                nc.scalar.activation(w1hi[:, k, :], raw[:, raw_slot(k), :], ACT.Copy).then_inc(w1hi_ready, 1)
                if k == 3:
                    act.wait_ge(m_done, 1)
                    for half in range(2):
                        nc.scalar.activation(m_sb[:, half * 512:(half + 1) * 512], bank[half][0:CONT, :],
                                             ACT.Copy).then_inc(m_ready, 1)
            act.wait_ge(par_in, 16)
            with act.Fori(0, BLOCKS) as b:
                act.wait_ge(cont_in, 16 * (b + 1))
                nc.scalar.activation(cont_sq[:, :], cont_sb[:, :], ACT.Square).then_inc(cont_sq_ready, 1)
                for g, (k0, k1) in enumerate(GROUPS):
                    for k in range(k0, k1):
                        s = k % XT
                        act.wait_ge(transposed, b * KT + (k + 1))
                        if k == 0:
                            act.wait_ge(acc_full, ACC_BANKS * b + EMPTY)
                        else:
                            act.wait_ge(x_used[s], X_USES[s] * b + (k // XT + EMPTY))
                        nc.scalar.activation(xhi[:, s, :], tp[k % TP], ACT.Copy).then_inc(xhi_ready, 1)
                    for j in range(BT):
                        rows = emb[:, j, :].rearrange("p (k c) -> p k c", c=PAIR)[:, k0:k1, 1:1 + P]
                        if j:
                            act.wait_ge(squared[g], BT * b + (j + EMPTY))
                        elif g:
                            act.wait_ge(squared[g - 1], BT * b + (BT + EMPTY))
                        else:
                            act.wait_ge(squared[-1], BT * b + EMPTY)
                        nc.scalar.activation(
                            junk[:, 0:(k1 - k0) * P].rearrange("p (k c) -> p k c", c=P), rows, ACT.Square,
                            accum_out=esq[:, ds(b * BT + j, 1), g]).then_inc(squared[g], 1)
                for m in range(ACC_BANKS):
                    act.wait_ge(acc_full, b * ACC_BANKS + (m + 1 + EMPTY))
                    for c in (2 * m, 2 * m + 1):
                        done = nc.scalar.activation(h1[:, c, ds(b * BC, BC)], acc[c], ACT.Identity,
                                                    bias=b1[:, c:c + 1])
                    done.then_inc(acc_free[m], 1)
            act.wait_ge(eps_ready, 1)
            nc.scalar.activation(warm[:, :], eps[:, :], ACT.Sqrt)
            act.wait_ge(bn1_step, C1)
            nc.scalar.activation(bn1[:, 0, :], mv1[:, :, 1], ACT.Sqrt, bias=eps[:, :]).then_inc(std1_ready, 1)
            act.wait_ge(bn1_step, C1 + 4)

            def evacuate(n):
                for m in range(C2):
                    act.wait_ge(acc2_full, n * C2 + m + 1)
                    nc.scalar.activation(h1[:, m, n * NB2:(n + 1) * NB2], bank[(n % 2) * C2 + m][:, :],
                                         ACT.Identity, bias=b2[:, m:m + 1]).then_inc(acc2_free, 1)

            for n in range(N2):
                for k in range(C1):
                    i = n * C1 + k
                    if i >= 2:
                        act.wait_ge(h_split, i - 1)
                    src = h1[:, k, n * NB2:(n + 1) * NB2]
                    nc.scalar.activation(hfull[:, i % 2, :], src, ACT.Relu, bias=bn1[:, 4, k:k + 1],
                                         scale=bn1[:, 2, k:k + 1])
                    if n >= 1:
                        if k < C1 - 1:
                            act.wait_ge(h_used[k], n)
                        else:
                            act.wait_ge(acc2_full, n * C2)
                    nc.scalar.activation(hhi[:, k, :], src, ACT.Relu, bias=bn1[:, 4, k:k + 1],
                                         scale=bn1[:, 2, k:k + 1]).then_inc(h_ready, 1)
                if n >= 1:
                    evacuate(n - 1)
            nc.scalar.activation(warm[:, :], eps[:, :], ACT.Sqrt)
            evacuate(N2 - 1)
            act.wait_ge(bn2_step, C2)
            nc.scalar.activation(bn2[:, 0, :], mv2[:, :, 1], ACT.Sqrt, bias=eps[:, :]).then_inc(std2_ready, 1)
            act.wait_ge(bn2_step, C2 + 4)
            for n in range(N2):
                for m in range(C2 // 2):
                    x = h1[:, m, n * NB2:(n + 1) * NB2]
                    nc.scalar.activation(x, x, ACT.Relu, bias=bn2[:, 4, m:m + 1],
                                         scale=bn2[:, 2, m:m + 1]).then_inc(out_act, 1)
            nc.scalar.activation(warm[:, :], eps[:, :], ACT.Sigmoid)
            act.wait_ge(z_ready, 1)
            nc.scalar.activation(prob[:, :, 1], zsum[:, :], ACT.Sigmoid).then_inc(prob_ready, 1)

        @block.vector
        def _(dve):
            for free in (*summed, *split_done, fm_step):
                dve.sem_inc(free, EMPTY)
            nc.vector.memset(eps[:, :], EPS).then_inc(eps_ready, 1)
            nc.vector.memset(idx_all[:, TILES * CAT:], 0)
            count = [0]

            def indices(ins):
                count[0] += 1
                ins.then_inc(idx_step, 1)
                dve.wait_ge(idx_step, count[0])

            n = TILES * CAT
            wrapped = emb[:, 0, 0:n]
            dve.wait_ge(idx_in, 16)
            indices(nc.vector.tensor_scalar(wrapped, idx_all[:, 0:n], 0, VOCAB, ALU.is_lt, ALU.mult))
            indices(nc.vector.tensor_tensor(wrapped, wrapped, idx_all[:, 0:n], ALU.add))
            indices(nc.vector.tensor_scalar(wrapped, wrapped, 0, VOCAB - 1, ALU.max, ALU.min))
            dve.wait_ge(off_made, 1)
            offsets = idx_off[:, :].unsqueeze(1).to_broadcast([P, TILES, CAT])
            indices(nc.vector.tensor_tensor(idx_all[:, 0:n].rearrange("p (t f) -> p t f", f=CAT),
                                            wrapped.rearrange("p (t f) -> p t f", f=CAT), offsets, ALU.add))

            def stage_indices(g, first_tile):
                k0, k1 = GROUPS[g]
                src = idx_all[:, :].rearrange("p (t f) -> p t f", f=CAT)
                nc.vector.tensor_copy(idx_now[:, :, 2 * k0:2 * k1],
                                      src[:, ds(first_tile, BT), 2 * k0:2 * k1]).then_inc(idx_ready[g], 1)

            for g in range(len(GROUPS)):
                stage_indices(g, 0)
            for k in range(KT):
                dve.wait_ge(w1hi_ready, k + 1)
                nc.vector.tensor_tensor(w1lo[:, k, :], raw[:, raw_slot(k), :], w1hi[:, k, :].bitcast(f32),
                                        ALU.subtract).then_inc(w1_ready, 1)
            with dve.Fori(0, BLOCKS) as b:
                for g, (k0, k1) in enumerate(GROUPS):
                    for k in range(k0, k1):
                        s = k % XT
                        dve.wait_ge(xhi_ready, b * KT + (k + 1))
                        nc.vector.tensor_tensor(xlo[:, s, :], tp[k % TP], xhi[:, s, :].bitcast(f32),
                                                ALU.subtract).then_inc(split_done[k % TP], 1)
                    rows = emb[:, :, :].rearrange("p j (k c) -> p j c k", c=PAIR)[:, :, :, k0:k1]
                    nc.vector.tensor_reduce(part[:, g, :].rearrange("p (j c) -> p j c", c=PAIR), rows,
                                            AX.X, ALU.add).then_inc(summed[g], 1)
                    stage_indices(g, (b + 1) * BT)
                for g in range(len(GROUPS)):
                    dve.wait_ge(summed[g], b + (1 + EMPTY))
                t = nc.vector.tensor_reduce(tot[:, :, :].rearrange("p j c -> p (j c)"),
                                            part[:, :, :].rearrange("p g c -> p c g"), AX.X, ALU.add)
                t.then_inc(fm_step, 1)
                dve.wait_ge(fm_step, FM_STEPS * b + (1 + EMPTY))
                nc.vector.tensor_tensor(ssum[:, :, :], tot[:, :, 1:1 + DIM], tot[:, :, 1 + DIM:1 + P],
                                        ALU.add).then_inc(fm_step, 1)
                nc.vector.tensor_tensor(lin0[:, :], tot[:, :, 0], tot[:, :, PAIR - 1],
                                        ALU.add).then_inc(fm_step, 1)
                dve.wait_ge(fm_step, FM_STEPS * b + (3 + EMPTY))
                dve.wait_ge(misc_full, b + 1)
                nc.vector.tensor_tensor(ssum[:, :, :], ssum[:, :, :], misc[:, :, 0:DIM],
                                        ALU.add).then_inc(fm_step, 1)
                nc.vector.tensor_tensor(lin1[:, :], lin0[:, :], misc[:, :, DIM], ALU.add).then_inc(fm_step, 1)
                dve.wait_ge(fm_step, FM_STEPS * b + (5 + EMPTY))
                nc.vector.tensor_tensor(ssum_sq[:, :, :], ssum[:, :, :], ssum[:, :, :],
                                        ALU.mult).then_inc(fm_step, 1)
                nc.vector.scalar_tensor_tensor(out=lin[:, ds(b * BT, BT)], in0=misc[:, :, DIM + 1], scalar=-0.5,
                                               in1=lin1[:, :], op0=ALU.mult, op1=ALU.add).then_inc(fm_step, 1)
                dve.wait_ge(fm_step, FM_STEPS * b + (7 + EMPTY))
                nc.vector.tensor_reduce(ssq[:, ds(b * BT, BT)], ssum_sq[:, :, :], AX.X,
                                        ALU.add).then_inc(fm_step, 1)
                for m in range(ACC_BANKS):
                    dve.wait_ge(acc_free[m], b + (1 + EMPTY))
                    for c in (2 * m, 2 * m + 1):
                        done = nc.vector.bn_stats(stats1[:, c, ds(b, 1), :].rearrange("p b s -> p (b s)"),
                                                  h1[:, c, ds(b * BC, BC)])
                done.then_inc(stats1_done, 1)
            dve.wait_ge(stats1_done, BLOCKS)
            for c in range(C1):
                nc.vector.bn_aggr(mv1[:, c, :], stats1[:, c, :, :].rearrange("p b s -> p (b s)")).then_inc(bn1_step, 1)

            def norm(bn, mv, g, be, step, first, std_ready):
                dve.wait_ge(step, first)
                dve.wait_ge(std_ready, 1)
                nc.vector.reciprocal(bn[:, 1, :], bn[:, 0, :]).then_inc(step, 1)
                dve.wait_ge(step, first + 1)
                nc.vector.tensor_tensor(bn[:, 2, :], g, bn[:, 1, :], ALU.mult).then_inc(step, 1)
                dve.wait_ge(step, first + 2)
                nc.vector.tensor_tensor(bn[:, 3, :], mv[:, :, 0], bn[:, 2, :], ALU.mult).then_inc(step, 1)
                dve.wait_ge(step, first + 3)
                nc.vector.tensor_tensor(bn[:, 4, :], be, bn[:, 3, :], ALU.subtract).then_inc(step, 1)

            norm(bn1, mv1, g1, be1, bn1_step, C1, std1_ready)

            def split_h(n):
                for k in range(C1):
                    i = n * C1 + k
                    dve.wait_ge(h_ready, i + 1)
                    nc.vector.tensor_tensor(hlo[:, k, :], hfull[:, i % 2, :], hhi[:, k, :].bitcast(f32),
                                            ALU.subtract).then_inc(h_split, 1)

            def stats(n):
                for m in range(C2):
                    dve.wait_ge(acc2_free, n * C2 + m + 1)
                    done = nc.vector.bn_stats(stats2[:, m, n, :], h1[:, m, n * NB2:(n + 1) * NB2])
                return done

            split_h(0)
            dve.wait_ge(fm_step, FM_STEPS * BLOCKS + EMPTY)
            for g in range(len(GROUPS)):
                dve.wait_ge(squared[g], BT * BLOCKS + EMPTY)
            nc.vector.tensor_reduce(esq_sum[:, :], esq[:, :, :], AX.X, ALU.add).then_inc(fin_step, 1)
            dve.wait_ge(fin_step, 1)
            nc.vector.tensor_tensor(fm_a[:, :], ssq[:, :], esq_sum[:, :], ALU.subtract).then_inc(fin_step, 1)
            dve.wait_ge(fin_step, 2)
            nc.vector.scalar_tensor_tensor(out=fm_b[:, :], in0=fm_a[:, :], scalar=0.5, in1=lin[:, :],
                                           op0=ALU.mult, op1=ALU.add).then_inc(fin_step, 1)
            dve.wait_ge(fin_step, 3)
            nc.vector.tensor_scalar(fm[:, :], fm_b[:, :], bias_col, b3_col, ALU.add, ALU.add).then_inc(fin_step, 1)
            for n in range(1, N2):
                split_h(n)
                stats(n - 1)
            stats(N2 - 1).then_inc(fin_step, 1)
            dve.wait_ge(fin_step, 5)
            for m in range(C2):
                nc.vector.bn_aggr(mv2[:, m, :], stats2[:, m, :, :].rearrange("p n s -> p (n s)")).then_inc(bn2_step, 1)
            norm(bn2, mv2, g2, be2, bn2_step, C2, std2_ready)
            dve.wait_ge(bn2_step, C2 + 4)
            tiles = [(n, m) for n in range(N2) for m in range(C2 // 2, C2)]
            for i, (n, m) in enumerate(tiles):
                x = h1[:, m, n * NB2:(n + 1) * NB2]
                nc.vector.tensor_scalar(x, x, bn2[:, 2, m:m + 1], bn2[:, 4, m:m + 1], ALU.mult,
                                        ALU.add).then_inc(out_dve, 1)
                dve.wait_ge(out_dve, 2 * i + 1)
                nc.vector.tensor_scalar(x, x, 0.0, None, ALU.max).then_inc(out_dve, 1)
            dve.wait_ge(logit_ready, 1)
            nc.vector.tensor_tensor(zsum[:, :], bank[0][:, 0:TILES], fm[:, :], ALU.add).then_inc(z_ready, 1)
            dve.wait_ge(prob_ready, 1)
            nc.vector.tensor_scalar(prob[:, :, 0], prob[:, :, 1], -1.0, 1.0, ALU.mult, ALU.add).then_inc(neg_ready, 1)

        @block.tensor
        def _(pe):
            for free in (cont_used, acc_full, *x_used):
                pe.sem_inc(free, EMPTY)
            pe.wait_ge(diag_in, 16)
            pe.wait_ge(wc_in, 32)
            for half in range(2):
                for j in range(CONT_KT):
                    rows = P if 2 * j + 1 < CONT else DIM
                    done = nc.tensor.matmul(bank[half][0:CONT, :], diag[0:rows, j * CONT:(j + 1) * CONT],
                                            raw[0:rows, j, half * 512:(half + 1) * 512],
                                            start=(j == 0), stop=(j == CONT_KT - 1))
            done.then_inc(m_done, 1)
            pe.wait_ge(ident_made, 1)
            pe.wait_ge(ctab_in, 16)
            pe.wait_ge(cnorm_ready, 1)
            pe.wait_ge(m_ready, 2)

            with pe.Fori(0, BLOCKS) as b:
                def transpose(k):
                    s = k % TP
                    pe.wait_ge(gathered[k], 16 * 2 * BT * (b + 1))
                    pe.wait_ge(split_done[s], TP_USES[s] * b + (k // TP + EMPTY))
                    for j in range(BT):
                        done = nc.tensor.transpose(tp[s][:, j * P:(j + 1) * P],
                                                   emb[:, j, k * PAIR + 1:k * PAIR + 1 + P], ident[:, :])
                    done.then_inc(transposed, 1)

                def multiply(k):
                    s = k % XT
                    pe.wait_ge(split_done[k % TP], TP_USES[k % TP] * b + (k // TP + 1 + EMPTY))
                    pe.wait_ge(w1_ready, k + 1)
                    last = k == KT - 1
                    for c in range(C1):
                        cols = slice(c * P, (c + 1) * P)
                        for n, (w, x) in enumerate(((w1hi, xhi), (w1hi, xlo), (w1lo, xhi))):
                            done = nc.tensor.matmul(acc[c], w[:, k, cols], x[:, s, :], start=False,
                                                    stop=(last and n == 2), skip_group_check=True)
                        if last and c % 2:
                            done.then_inc(acc_full, 1)
                    if not last:
                        done.then_inc(x_used[s], 1)

                transpose(0)
                pe.wait_ge(cont_in, 16 * (b + 1))
                pe.wait_ge(fm_step, FM_STEPS * b + EMPTY)
                pe.wait_ge(cont_sq_ready, b + 1)
                for j in range(BT):
                    cols = slice(j * P, (j + 1) * P)
                    nc.tensor.matmul(misc[:, j, 0:ROW], cont_sb[:, cols], ctab[:, :], start=True, stop=True)
                    done = nc.tensor.matmul(misc[:, j, ROW:ROW + 1], cont_sq[:, cols], cnorm[:, :],
                                            start=True, stop=True)
                done.then_inc(misc_full, 1)
                for c in range(C1):
                    if c % 2 == 0:
                        pe.wait_ge(acc_free[c // 2], b + EMPTY)
                    done = nc.tensor.matmul(acc[c], m_sb[:, c * P:(c + 1) * P], cont_sb[:, :],
                                            start=(c % 2 == 0), stop=False, skip_group_check=True)
                done.then_inc(cont_used, 1)
                for k in range(1, KT):
                    transpose(k)
                    multiply(k - 1)
                multiply(KT - 1)

            for n in range(N2):
                out2 = [bank[(n % 2) * C2 + m][:, :] for m in range(C2)]
                if n >= 2:
                    pe.wait_ge(acc2_free, (n - 1) * C2)
                for k in range(C1):
                    pe.wait_ge(h_split, n * C1 + k + 1)
                    pe.wait_ge(w2_ready, k + 1)
                    for m in range(C2):
                        cols = slice(m * P, (m + 1) * P)
                        for i, (w, x) in enumerate(((w2hi, hhi), (w2hi, hlo), (w2lo, hhi))):
                            done = nc.tensor.matmul(out2[m], w[:, k, cols], x[:, k, :],
                                                    start=(k == 0 and i == 0), stop=(k == C1 - 1 and i == 2))
                        if k == C1 - 1:
                            done.then_inc(acc2_full, 1)
                    if k < C1 - 1:
                        done.then_inc(h_used[k], 1)

            for n in range(N2):
                pe.wait_ge(out_act, (n + 1) * (C2 // 2))
                pe.wait_ge(out_dve, 2 * (n + 1) * (C2 // 2))
                for t in range(n * NB2 // P, (n + 1) * NB2 // P):
                    for m in range(C2):
                        done = nc.tensor.matmul(bank[0][:, t:t + 1], h1[:, m, t * P:(t + 1) * P], w3[:, m:m + 1],
                                                start=(m == 0), stop=(m == C2 - 1))
            done.then_inc(logit_ready, 1)


def kernel(**inputs):
    import numpy as np
    import concourse.bacc as bacc
    from concourse.bass_utils import run_bass_kernel_spmd

    x = {k.replace("L0_rec_", ""): np.asarray(v) for k, v in inputs.items()}

    table = np.empty((CAT, VOCAB, ROW), np.float32)
    table[0::2, :, 0], table[0::2, :, 1:] = x["cat_t1"][0::2], x["cat_t2"][0::2]
    table[1::2, :, DIM], table[1::2, :, :DIM] = x["cat_t1"][1::2], x["cat_t2"][1::2]

    cat = np.ascontiguousarray(x["r_cat_feats"].reshape(P, TILES * CAT))
    cont_t = np.ascontiguousarray(x["r_cont_feats"].reshape(P, TILES, CONT).transpose(2, 1, 0).reshape(CONT, BATCH))
    cont_tab = np.concatenate([x["cont_t2"], x["cont_t1"][:, None]], axis=1)
    cont_diag = np.zeros((P, CONT_KT, CONT), np.float32)
    for f in range(CONT):
        cont_diag[(f % 2) * DIM:(f % 2 + 1) * DIM, f // 2, f] = x["cont_t2"][f]
    cols = [x[n].reshape(-1, P).T for n in ("b1", "g1", "be1", "b2", "g2", "be2", "W3")]
    cols += [np.broadcast_to(x[n].reshape(1, 1), (P, 1)) for n in ("bias", "b3")]
    arrays = {
        "table": table.reshape(CAT * VOCAB, ROW), "cat": cat, "cont_t": cont_t, "cont_tab": cont_tab,
        "cont_diag": cont_diag.reshape(P, CONT_KT * CONT), "w1": x["W1"], "w2": x["W2"],
        "params": np.concatenate(cols, axis=1),
    }
    arrays = {f"in_{k}": np.ascontiguousarray(v) for k, v in arrays.items()}

    nc = bacc.Bacc("TRN2", target_bir_lowering=False, num_devices=1)
    args = [nc.dram_tensor(k, v.shape, mybir.dt.from_np(v.dtype), kind="ExternalInput").ap()
            for k, v in arrays.items()]
    out = nc.dram_tensor("out", (BATCH, 2), mybir.dt.float32, kind="ExternalOutput").ap()
    build(nc, *args, out.rearrange("(p t) c -> p (t c)", p=P))
    r = run_bass_kernel_spmd(nc, [arrays], core_ids=[0])
    return r.results[0]["out"]
```

```python
from contextlib import ExitStack

import concourse.bass as bass
from concourse import mybir

BATCH, CAT, CONT, VOCAB, DIM = 2048, 26, 13, 12500, 64
H1, H2 = 1024, 512
P = 128
EPS = 1e-5

TILES = BATCH // P
BT = 2
BLOCKS = TILES // BT
BC = BT * P
KT = CAT // 2
ROW = DIM + 1
PAIR = 2 * ROW
GROUPS = [(0, 4), (4, 8), (8, KT)]
C1 = H1 // P
C2 = H2 // P
ACC_BANKS = C1 * BC // 512
XT = 4
TP = 3
CONT_KT = -(-CONT // 2)
NB2 = 512
N2 = BATCH // NB2

EMPTY = 1
NORM_PARTS = [(0, 2), (2, C1)]
FM_STEPS = 8
PAR = 3 * C1 + 4 * C2 + 2


def build(nc, table, cat, cont_t, cont_tab, cont_diag, w1, w2, params, out):
    f32, f32r = mybir.dt.float32, mybir.dt.float32r
    i32, bf16 = mybir.dt.int32, mybir.dt.bfloat16
    ACT, ALU, AX = mybir.ActivationFunctionType, mybir.AluOpType, mybir.AxisListType
    ds = bass.ds

    base = -(-nc.sbuf_base // 32) * 32
    cursor = [base]

    def place(name, shape, dtype, size=4):
        n = size
        for d in shape[1:]:
            n *= d
        t = nc.alloc_sbuf_tensor_at(name, shape, dtype, offset=cursor[0])
        cursor[0] += -(-n // 32) * 32
        assert cursor[0] <= nc.sbuf_usable_end, (name, cursor[0])
        return t

    w1hi_at = cursor[0]
    w1hi = place("w1hi", [P, KT, H1], f32r)
    w1lo_at = cursor[0]
    w1lo = place("w1lo", [P, KT, H1], f32r)
    h1 = place("h1", [P, C1, BATCH], f32)
    emb = place("emb", [P, BT, KT * PAIR], f32)
    xhi = place("xhi", [P, XT, BC], f32r)
    xlo = place("xlo", [P, XT, BC], f32r)
    m_sb = place("m_sb", [CONT, H1], f32)
    cont_sb = place("cont_sb", [CONT, BC], f32)
    cont_sq = place("cont_sq", [CONT, BC], f32)
    ctab = place("ctab", [CONT, ROW], f32)
    ctab_sq = place("ctab_sq", [CONT, DIM], f32)
    cnorm = place("cnorm", [CONT, 1], f32)
    diag = place("diag", [P, CONT_KT * CONT], f32)
    idx_all = place("idx_all", [P, TILES * CAT], i32)
    idx_off = place("idx_off", [P, CAT], i32)
    idx_now = place("idx_now", [P, BT, CAT], i32)
    ident = place("ident", [P, P], f32)
    par = place("par", [P, PAR], f32)
    part = place("part", [P, len(GROUPS), BT * PAIR], f32)
    junk = place("junk", [P, (KT - 8) * P], bf16, 2)
    misc_sb = place("misc_sb", [P, BT, ROW + 1], f32)
    tot = place("tot", [P, BT, PAIR], f32)
    ssum = place("ssum", [P, BT, DIM], f32)
    ssum_sq = place("ssum_sq", [P, BT, DIM], f32)
    lin0 = place("lin0", [P, BT], f32)
    lin1 = place("lin1", [P, BT], f32)
    lin = place("lin", [P, TILES], f32)
    ssq = place("ssq", [P, TILES], f32)
    esq = place("esq", [P, TILES, len(GROUPS)], f32)
    eps = place("eps", [P, 1], f32)
    warm = place("warm", [P, 1], f32)
    stats1 = place("stats1", [P, C1, BLOCKS, 6], f32)
    mv1 = place("mv1", [P, C1, 2], f32)
    bn1 = place("bn1", [P, 5, C1], f32)

    kt_bytes = H1 * 4
    w2raw = nc.alloc_sbuf_tensor_at("w2raw", [P, C1, H2], f32, offset=w1hi_at)
    w2hi = nc.alloc_sbuf_tensor_at("w2hi", [P, C1, H2], f32r, offset=w1lo_at)
    w2lo = nc.alloc_sbuf_tensor_at("w2lo", [P, C1, H2], f32r, offset=w1lo_at + 4 * kt_bytes)
    hhi = nc.alloc_sbuf_tensor_at("hhi", [P, C1, NB2], f32r, offset=w1hi_at + 4 * kt_bytes)
    hlo = nc.alloc_sbuf_tensor_at("hlo", [P, C1, NB2], f32r, offset=w1lo_at + 8 * kt_bytes)
    hfull = nc.alloc_sbuf_tensor_at("hfull", [P, 2, NB2], f32, offset=w1hi_at + 8 * kt_bytes)
    cursor[0] = w1hi_at + 9 * kt_bytes
    esq_sum = place("esq_sum", [P, TILES], f32)
    fm_a = place("fm_a", [P, TILES], f32)
    fm_b = place("fm_b", [P, TILES], f32)
    fm = place("fm", [P, TILES], f32)
    stats2 = place("stats2", [P, C2, N2, 6], f32)
    mv2 = place("mv2", [P, C2, 2], f32)
    bn2 = place("bn2", [P, 5, C2], f32)
    zsum = place("zsum", [P, TILES], f32)
    prob = place("prob", [P, TILES, 2], f32)
    zpart = place("zpart", [P, TILES], f32)
    W2RAW_KT, W2LO_KT = 3, 7

    raw = h1[:, :, :].rearrange("p c (s n) -> p (c s) n", n=H1)
    RAW_SLOTS = C1 * BATCH // H1

    def raw_slot(k):
        return CONT_KT + k if k < RAW_SLOTS - CONT_KT else k - (RAW_SLOTS - CONT_KT)

    STD, RSTD, SCALE, MEAN_SCALE, SHIFT = range(5)

    b1, g1, be1 = (par[:, i * C1:(i + 1) * C1] for i in range(3))
    b2, g2, be2, w3 = (par[:, 3 * C1 + i * C2:3 * C1 + (i + 1) * C2] for i in range(4))
    bias_col, b3_col = par[:, PAR - 2:PAR - 1], par[:, PAR - 1:PAR]

    with ExitStack() as ctx:
        bank = [ctx.enter_context(nc.psum_tensor(f"bank{i}", [P, 512], f32)) for i in range(8)]
        acc = [bank[c * BC // 512][:, c * BC % 512:c * BC % 512 + BC] for c in range(C1)]
        tp = [bank[ACC_BANKS + i][:, 0:BC] for i in range(TP)]
        misc = bank[7][:, 0:BT * 128].rearrange("p (j c) -> p j c", j=BT)

        def sem(name):
            return ctx.enter_context(nc.semaphore(name))

        idx_in, par_in, diag_in, ctab_in = sem("idx_in"), sem("par_in"), sem("diag_in"), sem("ctab_in")
        wc_in = sem("wc_in")
        raw_in = [sem(f"raw_in{k}") for k in range(KT)]
        cont_in = sem("cont_in")
        off_made, ident_zero, ident_made = sem("off_made"), sem("ident_zero"), sem("ident_made")
        idx_step = sem("idx_step")
        idx_ready = [sem(f"idx_ready{g}") for g in range(len(GROUPS))]
        gathered = [sem(f"gathered{k}") for k in range(KT)]
        group_open = sem("group_open")
        m_done, m_ready = sem("m_done"), sem("m_ready")
        cnorm_ready, cont_sq_ready, cont_used = sem("cnorm_ready"), sem("cont_sq_ready"), sem("cont_used")
        w1hi_ready, w1_ready = sem("w1hi_ready"), sem("w1_ready")
        transposed, xhi_ready = sem("transposed"), sem("xhi_ready")
        split_done = [sem(f"split_done{s}") for s in range(TP)]
        x_used = [sem(f"x_used{s}") for s in range(XT)]
        acc_full = sem("acc_full")
        acc_free = [sem(f"acc_free{m}") for m in range(ACC_BANKS)]
        squared = [sem(f"squared{g}") for g in range(len(GROUPS))]
        summed = [sem(f"summed{g}") for g in range(len(GROUPS))]
        misc_full, misc_read = sem("misc_full"), sem("misc_read")
        fm_step = sem("fm_step")
        stats1_done, mean1_ready = sem("stats1_done"), sem("mean1_ready")
        std1_ready, norm1_ready = sem("std1_ready"), sem("norm1_ready")
        norm_step = sem("norm_step")
        eps_ready = sem("eps_ready")
        w2_in, w2hi_ready, w2_ready = sem("w2_in"), sem("w2hi_ready"), sem("w2_ready")
        h_high, h_full, h_split = sem("h_high"), sem("h_full"), sem("h_split")
        h_used = [sem(f"h_used{k}") for k in range(C1 - 1)]
        acc2_full, acc2_free = sem("acc2_full"), sem("acc2_free")
        stats2_done, mean2_ready = sem("stats2_done"), sem("mean2_ready")
        std2_ready, norm2_ready = sem("std2_ready"), sem("norm2_ready")
        fin_step = sem("fin_step")
        out2_ready, u_ready = sem("out2_ready"), sem("u_ready")
        z_transposed, z_ready, prob_ready, neg_ready = (
            sem("z_transposed"), sem("z_ready"), sem("prob_ready"), sem("neg_ready"))
        out_done = sem("out_done")

        TP_USES = [len(range(s, KT, TP)) for s in range(TP)]
        X_USES = [len(range(s, KT - 1, XT)) for s in range(XT)]

        def bank2(n, m):
            return bank[(n + 1) % 2 * C2 + m][:, :]

        W2HI_AT = {8: (0, 1), 9: (2, 3), 10: (4, 5), 11: (6, 7)}
        W2LO_AT = {9: (0, 1), 10: (2, 3, 4), 11: (5, 6, 7)}

        block = ctx.enter_context(nc.Block())

        @block.sync
        def _(sp):
            sp.dma_start(idx_all[:, :], cat).then_inc(idx_in, 16)
            rows = w1[CAT * DIM:, :]
            whole = (CONT_KT - 1) * P
            sp.dma_start(raw[:, 0:CONT_KT - 1, :],
                         rows[0:whole, :].rearrange("(j p) n -> p j n", p=P)).then_inc(wc_in, 16)
            sp.dma_start(raw[0:DIM, CONT_KT - 1, :], rows[whole:whole + DIM, :]).then_inc(wc_in, 16)
            for k in range(KT):
                if k == RAW_SLOTS - CONT_KT:
                    sp.wait_ge(m_done, 1)
                sp.dma_start(raw[:, raw_slot(k), :], w1[k * P:(k + 1) * P, :]).then_inc(raw_in[k], 16)
            with sp.Fori(0, BLOCKS) as b:
                sp.wait_ge(cont_used, b + EMPTY)
                sp.dma_start(cont_sb[:, :], cont_t[:, ds(b * BC, BC)]).then_inc(cont_in, 16)
            s = W2RAW_KT % XT
            sp.wait_ge(x_used[s], X_USES[s] * (BLOCKS - 1) + W2RAW_KT // XT + 1 + EMPTY)
            for k in range(C1):
                sp.dma_start(w2raw[:, k, :], w2[k * P:(k + 1) * P, :]).then_inc(w2_in, 16)
            sp.wait_ge(neg_ready, 1)
            sp.wait_ge(prob_ready, 1)
            sp.dma_start(out, prob[:, :, :].rearrange("p t c -> p (t c)")).then_inc(out_done, 16)
            sp.wait_ge(out_done, 16)

        @block.gpsimd
        def _(pool):
            nc.gpsimd.iota(idx_off[:, :], pattern=[[VOCAB, CAT]], base=0,
                           channel_multiplier=0).then_inc(off_made, 1)
            nc.gpsimd.memset(ident[:, :], 1.0).then_inc(ident_zero, 1)
            pool.wait_ge(ident_zero, 1)
            nc.gpsimd.affine_select(out=ident[:, :], in_=ident[:, :], compare_op=ALU.is_equal, fill=0.0,
                                    base=0, pattern=[[-1, P]], channel_multiplier=1).then_inc(ident_made, 1)
            with pool.Fori(0, BLOCKS) as b:
                for g, (k0, k1) in enumerate(GROUPS):
                    pool.wait_ge(idx_ready[g], b + 1)
                    pool.wait_ge(summed[g], b + EMPTY)
                    pool.wait_ge(squared[g], BT * b + EMPTY)
                    pool.sem_inc(group_open, 1)
                    for k in range(k0, k1):
                        for j in range(BT):
                            for half in range(2):
                                at = k * PAIR + half * ROW
                                f = 2 * k + half
                                nc.gpsimd.indirect_dma_start(
                                    out=emb[:, j, at:at + ROW], out_offset=None, in_=table,
                                    in_offset=bass.IndirectOffsetOnAxis(ap=idx_now[:, j, f:f + 1], axis=0),
                                ).then_inc(gathered[k], 16)

        @block.scalar
        def _(act):
            act.dma_start(diag[:, :], cont_diag).then_inc(diag_in, 16)
            act.dma_start(ctab[:, :], cont_tab).then_inc(ctab_in, 16)
            act.dma_start(par[:, :], params).then_inc(par_in, 16)
            for free in (*squared, *acc_free):
                act.sem_inc(free, EMPTY)
            act.wait_ge(ctab_in, 16)
            nc.scalar.activation(ctab_sq[:, :], ctab[:, 0:DIM], ACT.Square,
                                 accum_out=cnorm[:, :]).then_inc(cnorm_ready, 1)
            for k in range(KT):
                act.wait_ge(raw_in[k], 16)
                nc.scalar.activation(w1hi[:, k, :], raw[:, raw_slot(k), :], ACT.Copy).then_inc(w1hi_ready, 1)
                if k == 3:
                    act.wait_ge(m_done, 1)
                    for half in range(2):
                        nc.scalar.activation(m_sb[:, half * 512:(half + 1) * 512], bank[half][0:CONT, :],
                                             ACT.Copy).then_inc(m_ready, 1)
            act.wait_ge(par_in, 16)

            def x_high(b, k):
                s = k % XT
                act.wait_ge(transposed, b * KT + (k + 1))
                if k == 0:
                    act.wait_ge(acc_full, ACC_BANKS * b + EMPTY)
                else:
                    act.wait_ge(x_used[s], X_USES[s] * b + (k // XT + EMPTY))
                nc.scalar.activation(xhi[:, s, :], tp[k % TP], ACT.Copy).then_inc(xhi_ready, 1)

            def square(b, g):
                k0, k1 = GROUPS[g]
                for j in range(BT):
                    rows = emb[:, j, :].rearrange("p (k c) -> p k c", c=PAIR)[:, k0:k1, 1:1 + P]
                    if j:
                        act.wait_ge(squared[g], BT * b + (j + EMPTY))
                    elif g:
                        act.wait_ge(squared[g - 1], BT * b + (BT + EMPTY))
                    else:
                        act.wait_ge(squared[-1], BT * b + EMPTY)
                    nc.scalar.activation(
                        junk[:, 0:(k1 - k0) * P].rearrange("p (k c) -> p k c", c=P), rows, ACT.Square,
                        accum_out=esq[:, ds(b * BT + j, 1), g]).then_inc(squared[g], 1)

            def sums_out(b, m):
                act.wait_ge(acc_full, b * ACC_BANKS + (m + 1 + EMPTY))
                for c in (2 * m, 2 * m + 1):
                    done = nc.scalar.activation(h1[:, c, ds(b * BC, BC)], acc[c], ACT.Identity,
                                                bias=b1[:, c:c + 1])
                done.then_inc(acc_free[m], 1)

            def cont_squares(b):
                act.wait_ge(cont_in, 16 * (b + 1))
                nc.scalar.activation(cont_sq[:, :], cont_sb[:, :], ACT.Square).then_inc(cont_sq_ready, 1)

            with act.Fori(0, BLOCKS - 1) as b:
                cont_squares(b)
                for g, (k0, k1) in enumerate(GROUPS):
                    for k in range(k0, k1):
                        x_high(b, k)
                    square(b, g)
                for m in range(ACC_BANKS):
                    sums_out(b, m)

            b = BLOCKS - 1
            cont_squares(b)
            for g, (k0, k1) in enumerate(GROUPS):
                for k in range(k0, k1):
                    x_high(b, k)
                    if k in W2HI_AT:
                        act.wait_ge(w2_in, 16 * C1)
                        for i in W2HI_AT[k]:
                            nc.scalar.activation(w2hi[:, i, :], w2raw[:, i, :], ACT.Copy).then_inc(w2hi_ready, 1)
                if g < len(GROUPS) - 1:
                    square(b, g)
            act.wait_ge(eps_ready, 1)
            nc.scalar.activation(warm[:, :], eps[:, :], ACT.Sqrt)

            def std(bn, mv, lo, hi, mean_ready, std_ready):
                act.wait_ge(mean_ready, hi)
                nc.scalar.activation(bn[:, STD, lo:hi], mv[:, lo:hi, 1], ACT.Sqrt,
                                     bias=eps[:, :]).then_inc(std_ready, 1)

            def hidden(n, k):
                i = n * C1 + k
                src = h1[:, k, n * NB2:(n + 1) * NB2]
                shift, scale = bn1[:, SHIFT, k:k + 1], bn1[:, SCALE, k:k + 1]
                if n >= 1:
                    if k < C1 - 1:
                        act.wait_ge(h_used[k], n)
                    else:
                        act.wait_ge(acc2_full, n * C2)
                nc.scalar.activation(hhi[:, k, :], src, ACT.Relu, bias=shift, scale=scale).then_inc(h_high, 1)
                if i >= 2:
                    act.wait_ge(h_split, i - 1)
                nc.scalar.activation(hfull[:, i % 2, :], src, ACT.Relu, bias=shift,
                                     scale=scale).then_inc(h_full, 1)

            def sums2_out(n, m):
                act.wait_ge(acc2_full, n * C2 + m + 1)
                nc.scalar.activation(h1[:, m, n * NB2:(n + 1) * NB2], bank2(n, m), ACT.Identity,
                                     bias=b2[:, m:m + 1]).then_inc(acc2_free, 1)

            early = NORM_PARTS[0][1]
            sums_out(b, 0)
            sums_out(b, 1)
            std(bn1, mv1, *NORM_PARTS[0], mean1_ready, std1_ready)
            act.wait_ge(norm1_ready, 1)
            for k in range(early):
                hidden(0, k)
            sums_out(b, 2)
            sums_out(b, 3)
            std(bn1, mv1, *NORM_PARTS[1], mean1_ready, std1_ready)
            act.wait_ge(norm1_ready, 2)
            for k in range(early, C1):
                hidden(0, k)
            square(b, len(GROUPS) - 1)
            for n in range(1, N2):
                for k in range(C1):
                    hidden(n, k)
                for m in range(C2):
                    sums2_out(n - 1, m)
            for m in range(C2):
                sums2_out(N2 - 1, m)
                std(bn2, mv2, m, m + 1, mean2_ready, std2_ready)
                act.wait_ge(norm2_ready, m + 1)
                for n in range(N2):
                    x = h1[:, m, n * NB2:(n + 1) * NB2]
                    nc.scalar.activation(x, x, ACT.Relu, bias=bn2[:, SHIFT, m:m + 1],
                                         scale=bn2[:, SCALE, m:m + 1]).then_inc(out2_ready, 1)
            nc.scalar.activation(warm[:, :], eps[:, :], ACT.Sigmoid)
            act.wait_ge(z_ready, 1)
            nc.scalar.activation(prob[:, :, 1], zsum[:, :], ACT.Sigmoid).then_inc(prob_ready, 1)

        @block.vector
        def _(dve):
            for free in (*summed, *split_done, misc_read, fm_step):
                dve.sem_inc(free, EMPTY)
            nc.vector.memset(eps[:, :], EPS).then_inc(eps_ready, 1)
            count = [0]

            def counted(ins):
                count[0] += 1
                ins.then_inc(idx_step, 1)
                dve.wait_ge(idx_step, count[0])

            def find_rows(t0, t1):
                cols = slice(t0 * CAT, t1 * CAT)
                x = idx_all[:, cols]
                w = emb[:, 1, GROUPS[1][0] * PAIR:][:, cols]
                counted(nc.vector.tensor_scalar(w, x, 0, VOCAB, ALU.is_lt, ALU.mult))
                counted(nc.vector.tensor_tensor(w, w, x, ALU.add))
                counted(nc.vector.tensor_scalar(w, w, 0, VOCAB - 1, ALU.max, ALU.min))
                dve.wait_ge(off_made, 1)
                counted(nc.vector.tensor_tensor(x.rearrange("p (t f) -> p t f", f=CAT),
                                                w.rearrange("p (t f) -> p t f", f=CAT),
                                                idx_off[:, :].unsqueeze(1).to_broadcast([P, t1 - t0, CAT]),
                                                ALU.add))

            def stage_indices(g, first_tile):
                k0, k1 = GROUPS[g]
                src = idx_all[:, :].rearrange("p (t f) -> p t f", f=CAT)
                nc.vector.tensor_copy(idx_now[:, :, 2 * k0:2 * k1],
                                      src[:, ds(first_tile, BT), 2 * k0:2 * k1]).then_inc(idx_ready[g], 1)

            dve.wait_ge(idx_in, 16)
            find_rows(0, BT)
            stage_indices(0, 0)
            find_rows(BT, TILES)
            for g in range(1, len(GROUPS)):
                stage_indices(g, 0)
            for k in range(KT):
                dve.wait_ge(w1hi_ready, k + 1)
                nc.vector.tensor_tensor(w1lo[:, k, :], raw[:, raw_slot(k), :], w1hi[:, k, :].bitcast(f32),
                                        ALU.subtract).then_inc(w1_ready, 1)

            def x_low(b, k):
                s = k % XT
                dve.wait_ge(xhi_ready, b * KT + (k + 1))
                nc.vector.tensor_tensor(xlo[:, s, :], tp[k % TP], xhi[:, s, :].bitcast(f32),
                                        ALU.subtract).then_inc(split_done[k % TP], 1)

            def group_sum(b, g):
                k0, k1 = GROUPS[g]
                rows = emb[:, :, :].rearrange("p j (k c) -> p j c k", c=PAIR)[:, :, :, k0:k1]
                nc.vector.tensor_reduce(part[:, g, :].rearrange("p (j c) -> p j c", c=PAIR), rows,
                                        AX.X, ALU.add).then_inc(summed[g], 1)

            def keep_misc(b):
                dve.wait_ge(misc_full, b + 1)
                nc.vector.tensor_copy(misc_sb[:, :, :], misc[:, :, 0:ROW + 1]).then_inc(misc_read, 1)

            def fm_terms(b):
                def done_steps(n):
                    dve.wait_ge(fm_step, FM_STEPS * b + (n + EMPTY))

                for g in range(len(GROUPS)):
                    dve.wait_ge(summed[g], b + (1 + EMPTY))
                nc.vector.tensor_reduce(tot[:, :, :].rearrange("p j c -> p (j c)"),
                                        part[:, :, :].rearrange("p g c -> p c g"), AX.X,
                                        ALU.add).then_inc(fm_step, 1)
                done_steps(1)
                nc.vector.tensor_tensor(ssum[:, :, :], tot[:, :, 1:1 + DIM], tot[:, :, 1 + DIM:1 + P],
                                        ALU.add).then_inc(fm_step, 1)
                nc.vector.tensor_tensor(lin0[:, :], tot[:, :, 0], tot[:, :, PAIR - 1],
                                        ALU.add).then_inc(fm_step, 1)
                done_steps(3)
                dve.wait_ge(misc_read, b + (1 + EMPTY))
                nc.vector.tensor_tensor(ssum[:, :, :], ssum[:, :, :], misc_sb[:, :, 0:DIM],
                                        ALU.add).then_inc(fm_step, 1)
                nc.vector.tensor_tensor(lin1[:, :], lin0[:, :], misc_sb[:, :, DIM], ALU.add).then_inc(fm_step, 1)
                done_steps(5)
                nc.vector.tensor_tensor(ssum_sq[:, :, :], ssum[:, :, :], ssum[:, :, :],
                                        ALU.mult).then_inc(fm_step, 1)
                nc.vector.scalar_tensor_tensor(out=lin[:, ds(b * BT, BT)], in0=misc_sb[:, :, DIM + 1],
                                               scalar=-0.5, in1=lin1[:, :], op0=ALU.mult,
                                               op1=ALU.add).then_inc(fm_step, 1)
                done_steps(7)
                nc.vector.tensor_reduce(ssq[:, ds(b * BT, BT)], ssum_sq[:, :, :], AX.X,
                                        ALU.add).then_inc(fm_step, 1)

            def stats(b, m):
                dve.wait_ge(acc_free[m], b + (1 + EMPTY))
                for c in (2 * m, 2 * m + 1):
                    nc.vector.bn_stats(stats1[:, c, ds(b, 1), :].rearrange("p b s -> p (b s)"),
                                       h1[:, c, ds(b * BC, BC)]).then_inc(stats1_done, 1)

            with dve.Fori(0, BLOCKS - 1) as b:
                for g, (k0, k1) in enumerate(GROUPS):
                    for k in range(k0, k1):
                        x_low(b, k)
                        if k == 0:
                            keep_misc(b)
                    group_sum(b, g)
                    stage_indices(g, (b + 1) * BT)
                fm_terms(b)
                for m in range(ACC_BANKS):
                    stats(b, m)

            b = BLOCKS - 1
            for g, (k0, k1) in enumerate(GROUPS):
                for k in range(k0, k1):
                    x_low(b, k)
                    if k == 0:
                        keep_misc(b)
                    for i in W2LO_AT.get(k, ()):
                        if i == 0:
                            s = W2LO_KT % XT
                            dve.wait_ge(x_used[s], X_USES[s] * b + W2LO_KT // XT + 1 + EMPTY)
                        dve.wait_ge(w2hi_ready, i + 1)
                        nc.vector.tensor_tensor(w2lo[:, i, :], w2raw[:, i, :], w2hi[:, i, :].bitcast(f32),
                                                ALU.subtract).then_inc(w2_ready, 1)
                if g < len(GROUPS) - 1:
                    group_sum(b, g)

            steps = [0]

            def chained(ins):
                steps[0] += 1
                ins.then_inc(norm_step, 1)
                dve.wait_ge(norm_step, steps[0])

            def norm(bn, mv, g, be, lo, hi, std_ready, part_no, norm_ready):
                dve.wait_ge(std_ready, part_no + 1)
                chained(nc.vector.reciprocal(bn[:, RSTD, lo:hi], bn[:, STD, lo:hi]))
                chained(nc.vector.tensor_tensor(bn[:, SCALE, lo:hi], g[:, lo:hi], bn[:, RSTD, lo:hi], ALU.mult))
                chained(nc.vector.tensor_tensor(bn[:, MEAN_SCALE, lo:hi], mv[:, lo:hi, 0],
                                                bn[:, SCALE, lo:hi], ALU.mult))
                nc.vector.tensor_tensor(bn[:, SHIFT, lo:hi], be[:, lo:hi], bn[:, MEAN_SCALE, lo:hi],
                                        ALU.subtract).then_inc(norm_ready, 1)

            def norm1(part_no):
                lo, hi = NORM_PARTS[part_no]
                dve.wait_ge(stats1_done, C1 * b + hi)
                for c in range(lo, hi):
                    nc.vector.bn_aggr(mv1[:, c, :],
                                      stats1[:, c, :, :].rearrange("p b s -> p (b s)")).then_inc(mean1_ready, 1)
                dve.wait_ge(mean1_ready, hi)
                norm(bn1, mv1, g1, be1, lo, hi, std1_ready, part_no, norm1_ready)

            def h_low(n, k):
                i = n * C1 + k
                dve.wait_ge(h_full, i + 1)
                nc.vector.tensor_tensor(hlo[:, k, :], hfull[:, i % 2, :], hhi[:, k, :].bitcast(f32),
                                        ALU.subtract).then_inc(h_split, 1)

            def statistics2(n, m):
                dve.wait_ge(acc2_free, n * C2 + m + 1)
                nc.vector.bn_stats(stats2[:, m, n, :],
                                   h1[:, m, n * NB2:(n + 1) * NB2]).then_inc(stats2_done, 1)

            early = NORM_PARTS[0][1]
            stats(b, 0)
            norm1(0)
            stats(b, 1)
            for k in range(early):
                h_low(0, k)
            stats(b, 2)
            stats(b, 3)
            norm1(1)
            for k in range(early, C1):
                h_low(0, k)
            group_sum(b, len(GROUPS) - 1)
            fm_terms(b)
            dve.wait_ge(fm_step, FM_STEPS * BLOCKS + EMPTY)
            for g in range(len(GROUPS)):
                dve.wait_ge(squared[g], BT * BLOCKS + EMPTY)
            chained(nc.vector.tensor_reduce(esq_sum[:, :], esq[:, :, :], AX.X, ALU.add))
            chained(nc.vector.tensor_tensor(fm_a[:, :], ssq[:, :], esq_sum[:, :], ALU.subtract))
            chained(nc.vector.scalar_tensor_tensor(out=fm_b[:, :], in0=fm_a[:, :], scalar=0.5, in1=lin[:, :],
                                                   op0=ALU.mult, op1=ALU.add))
            chained(nc.vector.tensor_scalar(fm[:, :], fm_b[:, :], bias_col, b3_col, ALU.add, ALU.add))
            for n in range(1, N2):
                for k in range(C1):
                    h_low(n, k)
                for m in range(C2):
                    statistics2(n - 1, m)

            def z_sum(n):
                dve.wait_ge(z_transposed, n + 1)
                t0, t1 = n * NB2 // P, (n + 1) * NB2 // P
                chained(nc.vector.tensor_reduce(zpart[:, t0:t1],
                                                bank[C2 + n][:, :].rearrange("p (t c) -> p t c", c=P),
                                                AX.X, ALU.add))

            for m in range(C2):
                statistics2(N2 - 1, m)
                dve.wait_ge(stats2_done, (N2 - 1) * C2 + m + 1)
                nc.vector.bn_aggr(mv2[:, m, :],
                                  stats2[:, m, :, :].rearrange("p n s -> p (n s)")).then_inc(mean2_ready, 1)
                dve.wait_ge(mean2_ready, m + 1)
                norm(bn2, mv2, g2, be2, m, m + 1, std2_ready, m, norm2_ready)
                for n in range(N2):
                    cols = slice(n * NB2, (n + 1) * NB2)
                    u, x, w = h1[:, 0, cols], h1[:, m, cols], w3[:, m:m + 1]
                    dve.wait_ge(out2_ready, m * N2 + n + 1)
                    if m == 0:
                        nc.vector.tensor_scalar(u, x, w, None, ALU.mult).then_inc(u_ready, 1)
                    else:
                        dve.wait_ge(u_ready, (m - 1) * N2 + n + 1)
                        nc.vector.scalar_tensor_tensor(out=u, in0=x, scalar=w, in1=u, op0=ALU.mult,
                                                       op1=ALU.add).then_inc(u_ready, 1)
                    if m == C2 - 1 and n >= 1:
                        z_sum(n - 1)
            z_sum(N2 - 1)
            nc.vector.tensor_tensor(zsum[:, :], zpart[:, :], fm[:, :], ALU.add).then_inc(z_ready, 1)
            dve.wait_ge(prob_ready, 1)
            nc.vector.tensor_scalar(prob[:, :, 0], prob[:, :, 1], -1.0, 1.0, ALU.mult, ALU.add).then_inc(neg_ready, 1)

        @block.tensor
        def _(pe):
            for free in (cont_used, acc_full, *x_used):
                pe.sem_inc(free, EMPTY)
            pe.wait_ge(diag_in, 16)
            pe.wait_ge(wc_in, 32)
            for half in range(2):
                for j in range(CONT_KT):
                    rows = P if 2 * j + 1 < CONT else DIM
                    done = nc.tensor.matmul(bank[half][0:CONT, :], diag[0:rows, j * CONT:(j + 1) * CONT],
                                            raw[0:rows, j, half * 512:(half + 1) * 512],
                                            start=(j == 0), stop=(j == CONT_KT - 1))
            done.then_inc(m_done, 1)
            pe.wait_ge(ident_made, 1)
            pe.wait_ge(ctab_in, 16)
            pe.wait_ge(cnorm_ready, 1)
            pe.wait_ge(m_ready, 2)

            with pe.Fori(0, BLOCKS) as b:
                def transpose(k):
                    s = k % TP
                    pe.wait_ge(gathered[k], 16 * 2 * BT * (b + 1))
                    pe.wait_ge(split_done[s], TP_USES[s] * b + (k // TP + EMPTY))
                    for j in range(BT):
                        done = nc.tensor.transpose(tp[s][:, j * P:(j + 1) * P],
                                                   emb[:, j, k * PAIR + 1:k * PAIR + 1 + P], ident[:, :])
                    done.then_inc(transposed, 1)

                def multiply(k):
                    s = k % XT
                    pe.wait_ge(split_done[k % TP], TP_USES[k % TP] * b + (k // TP + 1 + EMPTY))
                    pe.wait_ge(w1_ready, k + 1)
                    last = k == KT - 1
                    for c in range(C1):
                        cols = slice(c * P, (c + 1) * P)
                        for n, (w, x) in enumerate(((w1hi, xhi), (w1hi, xlo), (w1lo, xhi))):
                            done = nc.tensor.matmul(acc[c], w[:, k, cols], x[:, s, :], start=False,
                                                    stop=(last and n == 2), skip_group_check=True)
                        if last and c % 2:
                            done.then_inc(acc_full, 1)
                    if not last:
                        done.then_inc(x_used[s], 1)

                transpose(0)
                pe.wait_ge(cont_in, 16 * (b + 1))
                pe.wait_ge(misc_read, b + EMPTY)
                pe.wait_ge(cont_sq_ready, b + 1)
                for j in range(BT):
                    cols = slice(j * P, (j + 1) * P)
                    nc.tensor.matmul(misc[:, j, 0:ROW], cont_sb[:, cols], ctab[:, :], start=True, stop=True)
                    done = nc.tensor.matmul(misc[:, j, ROW:ROW + 1], cont_sq[:, cols], cnorm[:, :],
                                            start=True, stop=True)
                done.then_inc(misc_full, 1)
                for c in range(C1):
                    if c % 2 == 0:
                        pe.wait_ge(acc_free[c // 2], b + EMPTY)
                    done = nc.tensor.matmul(acc[c], m_sb[:, c * P:(c + 1) * P], cont_sb[:, :],
                                            start=(c % 2 == 0), stop=False, skip_group_check=True)
                done.then_inc(cont_used, 1)
                for k in range(1, KT):
                    transpose(k)
                    multiply(k - 1)
                multiply(KT - 1)

            terms = ((w2hi, hhi), (w2lo, hhi), (w2hi, hlo))

            def products(n, k, m, which):
                cols = slice(m * P, (m + 1) * P)
                for i in which:
                    w, x = terms[i]
                    done = nc.tensor.matmul(bank2(n, m), w[:, k, cols], x[:, k, :],
                                            start=(k == 0 and i == 0), stop=(k == C1 - 1 and i == 2))
                if k == C1 - 1 and i == 2:
                    done.then_inc(acc2_full, 1)
                return done

            for n in range(N2 - 1):
                if n == 1:
                    for m in range(ACC_BANKS):
                        pe.wait_ge(acc_free[m], BLOCKS + EMPTY)
                if n >= 2:
                    pe.wait_ge(acc2_free, (n - 1) * C2)
                for k in range(C1):
                    pe.wait_ge(h_high, n * C1 + k + 1)
                    pe.wait_ge(w2_ready, k + 1)
                    for m in range(C2):
                        products(n, k, m, (0, 1))
                    pe.wait_ge(h_split, n * C1 + k + 1)
                    for m in range(C2):
                        done = products(n, k, m, (2,))
                    if k < C1 - 1:
                        done.then_inc(h_used[k], 1)
            n = N2 - 1
            pe.wait_ge(acc2_free, (n - 1) * C2)
            for m in range(C2):
                for k in range(C1):
                    if m == 0:
                        pe.wait_ge(h_split, n * C1 + k + 1)
                    products(n, k, m, (0, 1, 2))

            for n in range(N2):
                pe.wait_ge(u_ready, (C2 - 1) * N2 + n + 1)
                for t in range(NB2 // P):
                    done = nc.tensor.transpose(bank[C2 + n][:, t * P:(t + 1) * P],
                                               h1[:, 0, n * NB2 + t * P:n * NB2 + (t + 1) * P], ident[:, :])
                done.then_inc(z_transposed, 1)


def kernel(**inputs):
    import numpy as np
    import concourse.bacc as bacc
    from concourse.bass_utils import run_bass_kernel_spmd

    x = {k.replace("L0_rec_", ""): np.asarray(v) for k, v in inputs.items()}

    table = np.empty((CAT, VOCAB, ROW), np.float32)
    table[0::2, :, 0], table[0::2, :, 1:] = x["cat_t1"][0::2], x["cat_t2"][0::2]
    table[1::2, :, DIM], table[1::2, :, :DIM] = x["cat_t1"][1::2], x["cat_t2"][1::2]

    cat = np.ascontiguousarray(x["r_cat_feats"].reshape(P, TILES * CAT))
    cont_t = np.ascontiguousarray(x["r_cont_feats"].reshape(P, TILES, CONT).transpose(2, 1, 0).reshape(CONT, BATCH))
    cont_tab = np.concatenate([x["cont_t2"], x["cont_t1"][:, None]], axis=1)
    cont_diag = np.zeros((P, CONT_KT, CONT), np.float32)
    for f in range(CONT):
        cont_diag[(f % 2) * DIM:(f % 2 + 1) * DIM, f // 2, f] = x["cont_t2"][f]
    cols = [x[n].reshape(-1, P).T for n in ("b1", "g1", "be1", "b2", "g2", "be2", "W3")]
    cols += [np.broadcast_to(x[n].reshape(1, 1), (P, 1)) for n in ("bias", "b3")]
    arrays = {
        "table": table.reshape(CAT * VOCAB, ROW), "cat": cat, "cont_t": cont_t, "cont_tab": cont_tab,
        "cont_diag": cont_diag.reshape(P, CONT_KT * CONT), "w1": x["W1"], "w2": x["W2"],
        "params": np.concatenate(cols, axis=1),
    }
    arrays = {f"in_{k}": np.ascontiguousarray(v) for k, v in arrays.items()}

    nc = bacc.Bacc("TRN2", target_bir_lowering=False, num_devices=1)
    args = [nc.dram_tensor(k, v.shape, mybir.dt.from_np(v.dtype), kind="ExternalInput").ap()
            for k, v in arrays.items()]
    out = nc.dram_tensor("out", (BATCH, 2), mybir.dt.float32, kind="ExternalOutput").ap()
    build(nc, *args, out.rearrange("(p t) c -> p (t c)", p=P))
    r = run_bass_kernel_spmd(nc, [arrays], core_ids=[0])
    return r.results[0]["out"]
```
